# Optimizing a Trainium2 kernel written in Bass

```python
import numpy as np
import jax
import jax.numpy as jnp

def _softmax(x, axis=-1):
    return jax.nn.softmax(x, axis=axis)

def _gelu(x):
    return jax.nn.gelu(x, approximate=True)

def _silu(x):
    return jax.nn.silu(x)

def _sigmoid(x):
    return jax.nn.sigmoid(x)

def _layernorm(x, axis=-1, eps=1e-05):
    m = jnp.mean(x, axis=axis, keepdims=True)
    v = jnp.var(x, axis=axis, keepdims=True)
    return (x - m) / jnp.sqrt(v + eps)

def _scatter_add(tgt, idx, src, axis=0):
    return tgt.at[idx].add(src)

def _segment_sum(src, seg, n):
    return jax.ops.segment_sum(src, seg, n)
kernel_name = 'mk_adj_resnorm_d1_adj_r2_58db30'

def setup_inputs(seed: int=0):
    np.random.seed(seed)
    _w = jnp.asarray

    def _rec_inputs():
        import jax
        import jax.numpy as jnp
        _gk = jax.random.key(seed)
        x = -9.806e-05 + 1 * jax.random.normal(jax.random.fold_in(_gk, 1), (4096, 64), jnp.float32)
        _w = (1.0 + jnp.arange(4096, dtype=jnp.float32)) ** (-0.5)
        _w = _w / _w.mean()
        _pij = jnp.clip(0.00390625 * _w[:, None] * _w[None, :], 0.0, 1.0)
        _a = jax.random.uniform(jax.random.fold_in(_gk, 2), (4096, 4096)) < _pij
        _af = _a.astype(jnp.float32)
        adj = _af
        return (x, adj)
    x, adj = _rec_inputs()

    def _L0_gnn_setup():
        import jax, jax.numpy as jnp
        import numpy as np
        N, D_IN, D_OUT = (4096, 64, 64)
        MAX_NEIGH = 100
        DECAY = 0.5
        key = jax.random.key(seed)
        k1, k2, k3, k4 = jax.random.split(key, 4)
        stdv = 1.0 / np.sqrt(D_OUT)
        inputs = {'input': jax.random.normal(k1, (N, D_IN), dtype=jnp.float32), 'adj': jax.random.randint(k2, (N, N), 0, 2).astype(jnp.float32), 'weight': jax.random.uniform(k3, (D_IN, D_OUT), minval=-stdv, maxval=stdv, dtype=jnp.float32), 'bias': jax.random.uniform(k4, (D_OUT,), minval=-stdv, maxval=stdv, dtype=jnp.float32)}
        return inputs
    _L0_gnn_all = _L0_gnn_setup()
    _L0_gnn_in = {k: v for k, v in _L0_gnn_all.items() if k in ('weight', 'bias')}
    del _L0_gnn_all
    return {'x': x, 'adj': adj, 'L0_gnn_weight': _L0_gnn_in['weight'], 'L0_gnn_bias': _L0_gnn_in['bias']}

def reference(x, adj, L0_gnn_weight, L0_gnn_bias):
    import jax
    import jax.numpy as jnp

    def _L0_gnn_ref(input, adj, weight, bias):
        import jax, jax.numpy as jnp
        import numpy as np
        N, D_IN, D_OUT = (4096, 64, 64)
        MAX_NEIGH = 100
        DECAY = 0.5
        support = input @ weight
        mask = (adj != 0).astype(support.dtype)
        rank = jnp.cumsum(mask, axis=1)
        deg = rank[:, -1:]
        k = jnp.minimum(deg, float(MAX_NEIGH))
        pos = rank - (deg - k)
        w = mask * jnp.where(pos > 0, DECAY ** (k - pos), 0.0)
        out = w @ support + bias
        return out
    x = _layernorm(x + _L0_gnn_ref(x, adj, L0_gnn_weight, L0_gnn_bias), axis=-1)
    return x

_drawn_inputs = setup_inputs


def setup_inputs(seed=0):
    import zlib

    import numpy as np

    out = dict(_drawn_inputs(seed))
    spreads = {}
    factors = {}
    for name, (base, spread) in spreads.items():
        noise = np.random.default_rng([zlib.crc32(name.encode()), seed]).standard_normal(out[name].shape)
        drawn = base * np.exp(spread * noise) if base else spread * noise
        out[name] = jnp.asarray(drawn.astype(out[name].dtype))
    for name, factor in factors.items():
        out[name] = (out[name] * factor).astype(out[name].dtype)
    return out
```

```python
import concourse.bass as bass
from concourse import mybir
from contextlib import ExitStack


def gnn_decay_resnorm_kernel(nc: bass.Bass, x: bass.AP, adj: bass.AP, weight: bass.AP, bias: bass.AP, out: bass.AP):
    fp32, bf16, i16 = mybir.dt.float32, mybir.dt.bfloat16, mybir.dt.int16
    ALU = mybir.AluOpType
    ACT = mybir.ActivationFunctionType
    AX = mybir.AxisListType

    P = 128
    N, D = x.shape
    MAX_NEIGH = 100
    EPS = 1e-5
    LSB = 128
    REAL, CARRY, ONES = P - 2, P - 2, P - 1
    NB = -(-N // REAL)
    PAD = NB * REAL
    TILES = N // P
    U = 4
    GROUPS = TILES // U
    CHUNK = [7, 7, 7, 6, 6]
    CH0 = [0, 7, 14, 21, 27]
    K = len(CHUNK)
    CW = max(CHUNK) * P
    BY_DVE = (1, 3)
    RING = 4
    LAG = 3
    ABOVE = -LSB
    TAG = 2 ** 14
    SELF = TAG - LSB
    SCALE = 2.0 ** (127 - MAX_NEIGH)
    ONE0 = LSB * (MAX_NEIGH + 1) - TAG - (ABOVE * (REAL - 1) + SELF + ABOVE)
    assert sum(CHUNK) == NB and ONE0 == -28 * LSB

    x_rows = x.rearrange("(t p) d -> p t d", p=P)
    out_rows = out.rearrange("(t p) d -> p t d", p=P)

    ctx = ExitStack()
    with ctx:
        def sb(name, shape, dt):
            return ctx.enter_context(nc.sbuf_tensor(name, shape, dt))

        def pb(name, shape, dt):
            return ctx.enter_context(nc.psum_tensor(name, shape, dt))

        def sem(name):
            return ctx.enter_context(nc.semaphore(name))

        adj_sb = [sb(f"adj_sb{u}", [P, PAD], fp32) for u in range(U)]
        marks = [sb(f"marks{u}", [P, NB, P], bf16) for u in range(U)]
        marksT = [sb(f"marksT{n}", [P, CW], bf16) for n in range(RING)]
        weights = [sb(f"weights{n}", [P, CW], i16) for n in range(RING)]
        h64 = sb("h64", [P, NB, 64], bf16)
        h32 = sb("h32", [P, NB, 32], bf16)
        h16 = sb("h16", [P, NB, 16], bf16)
        h8 = sb("h8", [P, NB, 8], bf16)
        block_sum = sb("block_sum", [P, NB], fp32)
        c128 = sb("c128", [P, NB - 1], fp32)
        x_sb = sb("x_sb", [P, TILES, D], fp32)
        xT = sb("xT", [D, PAD], fp32)
        w_sb = sb("w_sb", [D, D], fp32)
        bias_sb = sb("bias_sb", [P, D], fp32)
        xb = sb("xb", [P, TILES, D], fp32)
        support = sb("support", [P, NB, D], fp32)
        rest = sb("rest", [P, NB, D], fp32)
        parts = sb("parts", [P, NB, 3, D], bf16)
        ident_f = sb("ident_f", [P, P], fp32)
        ident = sb("ident", [P, P], bf16)
        rule_f = sb("rule_f", [P, P], fp32)
        rule = sb("rule", [P, P], bf16)
        z = sb("z", [P, U, D], fp32)
        zx = sb("zx", [P, U, D], fp32)
        stats = sb("stats", [P, U, 6], fp32)
        mv = sb("mv", [P, U, 2], fp32)
        veps = sb("veps", [P, U], fp32)
        rstd = sb("rstd", [P, U], fp32)
        mhalf = sb("mhalf", [P, U], fp32)
        eps = sb("eps", [P, U], fp32)
        zeros = sb("zeros", [P, NB], fp32)
        ones = sb("ones", [P, NB], fp32)
        y = sb("y", [P, 2, U, D], fp32)

        tr_ps = [pb(f"tr_ps{n}", [P, 1024], bf16) for n in range(2)]
        bits_ps = pb("bits_ps", [P, 2, 1024], fp32)
        sum_ps = [pb(f"sum_ps{n}", [P, 512], fp32) for n in range(2)]
        flat_ps = bits_ps[:, :, :].rearrange("p a b -> p (a b)")
        sums = [sum_ps[n][:, 0:3 * D] for n in range(2)]

        adj_in = [sem(f"adj_in{u}") for u in range(U)]
        x_in, w_in, bias_in = sem("x_in"), sem("w_in"), sem("bias_in")
        out_done = [sem(f"out_done{n}") for n in range(2)]
        pool_step = sem("pool_step")
        consts = sem("consts")
        support_T = sem("support_T")
        xT_done = sem("xT_done")
        support_out = sem("support_out")
        split = sem("split")
        reset = sem("reset")
        masked = sem("masked")
        halved = sem("halved")
        carried = sem("carried")
        transposed = sem("transposed")
        marksT_act, marksT_dve = sem("marksT_act"), sem("marksT_dve")
        counted = sem("counted")
        weighed = sem("weighed")
        multiplied = sem("multiplied")
        summed = sem("summed")
        added = sem("added")
        bn1, bn2 = sem("bn1"), sem("bn2")
        norm = sem("norm")
        HSTEPS, NSTEPS = 5, 4

        block = ctx.enter_context(nc.Block())

        def act_copies(k):
            return len([n for n in range(k) if n not in BY_DVE])

        def dve_copies(k):
            return k - act_copies(k)

        def wait_marksT(eng, g, u, k):
            t = g * U + u
            if k in BY_DVE:
                eng.wait_ge(marksT_dve, t * dve_copies(K) + dve_copies(k + 1))
            else:
                eng.wait_ge(marksT_act, t * act_copies(K) + act_copies(k + 1))

        def back(g, u, k, lag):
            s = u * K + k - lag
            return g + s // (U * K), s // K % U, s % K

        @block.sync
        def _(sp):
            def load(g, u, first):
                if not first:
                    sp.wait_ge(masked, 2 * ((g - 1) * U + u + 1))
                sp.dma_start(adj_sb[u][:, 0:N], adj[bass.ds((g * U + u) * P, P), :]).then_inc(adj_in[u], 16)

            def store(g, half):
                sp.wait_ge(norm, NSTEPS * (g + 1))
                sp.dma_start(out_rows[:, bass.ds(g * U, U), :], y[:, half]).then_inc(out_done[half], 16)

            sp.dma_start(x_sb[:], x_rows).then_inc(x_in, 16)
            sp.dma_start(w_sb[:], weight).then_inc(w_in, 16)
            sp.dma_start(bias_sb[:], bias.rearrange("(o d) -> o d", o=1).broadcast_to([P, D])).then_inc(bias_in, 16)
            for u in range(U):
                load(0, u, True)
            for u in range(U):
                load(1, u, False)
            with sp.Fori(1, GROUPS // 2) as h:
                for i in range(2):
                    for u in range(U):
                        load(h * 2 + i, u, False)
                    store(h * 2 + i - 2, i)
            for i in range(2):
                store(GROUPS - 2 + i, i)
            for i in range(2):
                sp.wait_ge(out_done[i], 16 * GROUPS // 2)

        @block.gpsimd
        def _(pool):
            gp = nc.gpsimd
            n_step = [0]

            def step(ins):
                n_step[0] += 1
                ins.then_inc(pool_step, 1)

            def wait_steps():
                pool.wait_ge(pool_step, n_step[0])

            step(gp.memset(ident_f[:], 0.0))
            step(gp.iota(rule_f[:], pattern=[[-LSB, P]], base=ONE0, channel_multiplier=0,
                         allow_small_or_imprecise_dtypes=True))
            step(gp.memset(xT[:, N:PAD], 0.0))
            wait_steps()
            step(gp.affine_select(out=ident_f[:], in_=ident_f[:], compare_op=ALU.not_equal, fill=1.0, base=0,
                                  pattern=[[-1, P]], channel_multiplier=1))
            step(gp.affine_select(out=rule_f[:], in_=rule_f[:], compare_op=ALU.is_ge, fill=float(ABOVE), base=-ONES,
                                  pattern=[[0, P]], channel_multiplier=1))
            wait_steps()
            step(gp.affine_select(out=rule_f[:], in_=rule_f[:], compare_op=ALU.is_gt, fill=0.0, base=0,
                                  pattern=[[-1, P]], channel_multiplier=1))
            step(gp.tensor_copy(ident[:], ident_f[:]))
            wait_steps()
            step(gp.affine_select(out=rule_f[:], in_=rule_f[:], compare_op=ALU.not_equal, fill=float(SELF), base=0,
                                  pattern=[[-1, P]], channel_multiplier=1))
            wait_steps()
            step(gp.memset(rule_f[:, REAL:P], 0.0))
            wait_steps()
            gp.tensor_copy(rule[:], rule_f[:]).then_inc(consts, 1)
            for u in range(U):
                gp.memset(adj_sb[u][:, N:PAD], 0.0).then_inc(consts, 1)
                gp.memset(marks[u][:, :, CARRY:P], 1.0).then_inc(consts, 1)
            gp.memset(c128[:], float(P)).then_inc(consts, 1)
            gp.memset(parts[:], 0.0).then_inc(consts, 1)
            step(gp.memset(mhalf[:], -0.5))
            step(gp.memset(eps[:], EPS))
            step(gp.memset(zeros[:], 0.0))
            step(gp.memset(ones[:], 1.0))
            pool.wait_ge(consts, 2 * U + 3)
            R = REAL
            pool.wait_ge(support_out, 2)
            gp.tensor_copy(parts[0:R, :, 0, :], support[0:R]).then_inc(split, 1)
            pool.wait_ge(split, 1)
            gp.tensor_tensor(rest[0:R], support[0:R], parts[0:R, :, 0, :], ALU.subtract).then_inc(split, 1)
            pool.wait_ge(split, 2)
            gp.tensor_copy(parts[0:R, :, 1, :], rest[0:R]).then_inc(split, 1)
            pool.wait_ge(split, 3)
            gp.tensor_tensor(rest[0:R], rest[0:R], parts[0:R, :, 1, :], ALU.subtract).then_inc(split, 1)
            pool.wait_ge(split, 4)
            gp.tensor_copy(parts[0:R, :, 2, :], rest[0:R]).then_inc(split, 1)
            pool.wait_ge(x_in, 16)
            pool.wait_ge(bias_in, 16)
            step(gp.tensor_tensor(xb[:], x_sb[:], bias_sb[:, None, :].broadcast_to([P, TILES, D]), ALU.add))
            wait_steps()

            def normalise(g, half, stored):
                pool.wait_ge(summed, U * (g + 1))
                gp.tensor_tensor(zx[:], z[:], xb[:, bass.ds(g * U, U), :], ALU.add).then_inc(added, 1)
                pool.wait_ge(bn2, U * (g + 1))
                gp.tensor_tensor(veps[:], mv[:, :, 1], eps[:], ALU.add).then_inc(norm, 1)
                pool.wait_ge(norm, NSTEPS * g + 1)
                gp.tensor_tensor(rstd[:], veps[:], mhalf[:], ALU.pow).then_inc(norm, 1)
                if stored is not None:
                    pool.wait_ge(out_done[half], 16 * stored)
                gp.tensor_tensor(y[:, half], zx[:], mv[:, :, 0:1].broadcast_to([P, U, D]),
                                 ALU.subtract).then_inc(norm, 1)
                pool.wait_ge(norm, NSTEPS * g + 3)
                gp.tensor_tensor(y[:, half], y[:, half], rstd[:, :, None].broadcast_to([P, U, D]),
                                 ALU.mult).then_inc(norm, 1)

            def reset_carries(g):
                for u in range(U):
                    pool.wait_ge(transposed, K * (g * U + u + 1))
                    gp.tensor_tensor(marks[u][:, :, CARRY], zeros[:], ones[:], ALU.add).then_inc(reset, 1)

            reset_carries(0)
            normalise(0, 0, None)
            reset_carries(1)
            normalise(1, 1, None)
            with pool.Fori(1, GROUPS // 2) as h:
                for i in range(2):
                    reset_carries(h * 2 + i)
                    normalise(h * 2 + i, i, h)

        @block.tensor
        def _(pe):
            mm = nc.tensor.matmul
            pe.wait_ge(consts, 2 * U + 3)
            pe.wait_ge(x_in, 16)
            for h in range(2):
                if h:
                    pe.wait_ge(xT_done, h)
                for n in range(TILES // 2):
                    last = nc.tensor.transpose(flat_ps[0:D, n * P:(n + 1) * P], x_sb[:, h * TILES // 2 + n, :],
                                               ident_f[:])
                last.then_inc(support_T, 1)
            pe.wait_ge(w_in, 16)
            pe.wait_ge(xT_done, 2)
            for b in range(NB):
                dst = flat_ps[0:REAL, b * D:(b + 1) * D] if b < NB - 1 else sum_ps[0][0:REAL, 0:D]
                last = mm(dst, xT[:, b * REAL:(b + 1) * REAL], w_sb[:], start=True, stop=True)
            last.then_inc(support_T, 1)

            def transposes(g, u, k, first):
                if k == 0:
                    pe.wait_ge(carried, g * U + u + 1)
                s = u * K + k
                if s >= 2 or not first:
                    wait_marksT(pe, *back(g, u, k, 2))
                for n in range(CHUNK[k]):
                    last = nc.tensor.transpose(tr_ps[s % 2][:, n * P:(n + 1) * P],
                                               marks[u][:, CH0[k] + n, :], ident[:])
                last.then_inc(transposed, 1)

            def count(g, u, k, first):
                s = u * K + k
                wait_marksT(pe, g, u, k)
                if s >= 2 or not first:
                    pe.wait_ge(weighed, g * (U * K) + s - 1)
                else:
                    pe.wait_ge(support_out, 2)
                for c in range(0, CHUNK[k] * P, 512):
                    e = min(c + 512, CHUNK[k] * P)
                    last = mm(bits_ps[:, s % 2, c:e], rule[:], marksT[s % RING][:, c:e], start=True, stop=True)
                last.then_inc(counted, 1)

            def product(g, u, k, first):
                s = u * K + k
                pe.wait_ge(weighed, g * (U * K) + s + 1)
                if k == 0:
                    if u >= 2 or not first:
                        pe.wait_ge(summed, g * U + u - 1)
                    elif u == 0:
                        pe.wait_ge(split, 5)
                w = weights[s % RING][:].bitcast(bf16)
                for n in range(CHUNK[k]):
                    b = CH0[k] + n
                    last = mm(sums[u % 2], w[:, n * P:(n + 1) * P], parts[:, b].rearrange("p a d -> p (a d)"),
                              start=(b == 0), stop=(b == NB - 1))
                last.then_inc(multiplied, 1)

            def group(g, first):
                for u in range(U):
                    for k in range(K):
                        s = u * K + k
                        transposes(g, u, k, first)
                        for fn, lag in ((count, 1), (product, LAG)):
                            if s >= lag or not first:
                                fn(*back(g, u, k, lag), first and s >= lag)

            group(0, True)
            with pe.Fori(1, GROUPS) as g:
                group(g, False)
            for d in range(LAG):
                if d < 1:
                    count(GROUPS - 1, U - 1, K - 1, False)
                product(*back(GROUPS - 1, U - 1, K - 1, LAG - 1 - d), False)

        @block.scalar
        def _(act):
            H = N // 2
            for h in range(2):
                act.wait_ge(support_T, h + 1)
                nc.scalar.copy(xT[:, h * H:(h + 1) * H], flat_ps[0:D, 0:H]).then_inc(xT_done, 1)
            act.wait_ge(support_T, 3)
            nc.scalar.mul(support[0:REAL, 0:NB - 1, :].rearrange("p b d -> p (b d)"),
                          flat_ps[0:REAL, 0:(NB - 1) * D], SCALE).then_inc(support_out, 1)
            nc.scalar.mul(support[0:REAL, NB - 1, :], sum_ps[0][0:REAL, 0:D], SCALE).then_inc(support_out, 1)

            def copy_marks(g, u, k, first):
                s = u * K + k
                act.wait_ge(transposed, g * (U * K) + s + 1)
                if s >= RING or not first:
                    act.wait_ge(counted, g * (U * K) + s + 1 - RING)
                c = CHUNK[k] * P
                nc.scalar.copy(marksT[s % RING][:, 0:c].bitcast(fp32),
                               tr_ps[s % 2][:, 0:c].bitcast(fp32)).then_inc(marksT_act, 1)

            def weigh(g, u, k, first):
                s = u * K + k
                act.wait_ge(counted, g * (U * K) + s + 1)
                if s >= RING or not first:
                    act.wait_ge(multiplied, g * (U * K) + s + 1 - RING)
                c = CHUNK[k] * P
                nc.scalar.activation(weights[s % RING][:, 0:c], bits_ps[:, s % 2, 0:c],
                                     ACT.Relu).then_inc(weighed, 1)

            def group(g, first):
                for u in range(U):
                    for k in range(K):
                        if k not in BY_DVE:
                            copy_marks(g, u, k, first)
                        s = u * K + k
                        if s >= 1 or not first:
                            weigh(*back(g, u, k, 1), first and s >= 1)

            group(0, True)
            with act.Fori(1, GROUPS) as g:
                group(g, False)
            weigh(GROUPS - 1, U - 1, K - 1, False)

        @block.vector
        def _(dve):
            v = nc.vector
            HALF = NB // 2 + 1

            def mark(g, u, part, first):
                lo, hi = (0, HALF) if part == 0 else (HALF, NB)
                if part == 0:
                    dve.wait_ge(adj_in[u], 16 * (g + 1))
                    if not first:
                        dve.wait_ge(reset, (g - 1) * U + u + 1)
                v.tensor_scalar(marks[u][:, lo:hi, 0:REAL],
                                adj_sb[u][:, lo * REAL:hi * REAL].rearrange("p (b c) -> p b c", c=REAL),
                                0.0, 1.0, ALU.not_equal, ALU.add).then_inc(masked, 1)

            def block_sums(g, u, steps):
                t = g * U + u
                src = [marks[u], h64, h32, h16]
                dst = [h64, h32, h16, h8]
                for n in steps:
                    if n == 0:
                        dve.wait_ge(masked, 2 * t + 2)
                    else:
                        dve.wait_ge(halved, HSTEPS * t + n)
                    if n < 4:
                        w = 64 >> n
                        v.tensor_tensor(dst[n][:, :, :], src[n][:, :, 0:w], src[n][:, :, w:2 * w],
                                        ALU.add).then_inc(halved, 1)
                    elif n == 4:
                        v.tensor_reduce(block_sum[:], h8[:, :, :], AX.X, ALU.add).then_inc(halved, 1)
                    else:
                        v.tensor_tensor_scan(marks[u][:, NB - 2::-1, CARRY], block_sum[:, NB - 1:0:-1], c128[:],
                                             1.0, ALU.add, ALU.subtract).then_inc(carried, 1)

            def copy_marks(g, u, k, first):
                s = u * K + k
                dve.wait_ge(transposed, g * (U * K) + s + 1)
                if s >= RING or not first:
                    dve.wait_ge(counted, g * (U * K) + s + 1 - RING)
                c = CHUNK[k] * P
                v.tensor_copy(marksT[s % RING][:, 0:c].bitcast(fp32),
                              tr_ps[s % 2][:, 0:c].bitcast(fp32)).then_inc(marksT_dve, 1)

            def add_parts(g, u, first):
                dve.wait_ge(multiplied, K * (g * U + u + 1))
                if u == 0 and not first:
                    dve.wait_ge(added, g)
                v.tensor_reduce(z[:, u, :], sums[u % 2].rearrange("p (a d) -> p d a", a=3), AX.X,
                                ALU.add).then_inc(summed, 1)

            def statistics(g):
                dve.wait_ge(added, g + 1)
                for u in range(U):
                    v.bn_stats(stats[:, u, :], zx[:, u, :]).then_inc(bn1, 1)

            def wait_statistics(g):
                dve.wait_ge(bn1, U * (g + 1))

            def aggregate():
                for u in range(U):
                    v.bn_aggr(mv[:, u, :], stats[:, u, :]).then_inc(bn2, 1)

            def tile(g, u, first):
                tile0 = first and u == 0
                if u == 3 and not first:
                    wait_statistics(g - 1)
                mark(g, u, 0, first)
                if u == 3 and not first:
                    aggregate()
                if not tile0:
                    g1, u1 = (g, u - 1) if u else (g - 1, U - 1)
                    copy_marks(g1, u1, 1, first)
                mark(g, u, 1, first)
                block_sums(g, u, (0,))
                if not tile0:
                    copy_marks(g1, u1, 3, first)
                block_sums(g, u, (1, 2, 3, 4, 5))
                if not (first and u < 2):
                    add_parts(*((g, u - 2, first) if u >= 2 else (g - 1, u + 2, False)))
                if u == 2 and not first:
                    statistics(g - 1)

            dve.wait_ge(consts, 2 * U + 3)
            for u in range(U):
                tile(0, u, True)
            with dve.Fori(1, GROUPS) as g:
                for u in range(U):
                    tile(g, u, False)
            G = GROUPS - 1
            copy_marks(G, U - 1, 1, False)
            add_parts(G, U - 2, False)
            copy_marks(G, U - 1, 3, False)
            add_parts(G, U - 1, False)
            statistics(G)
            wait_statistics(G)
            aggregate()


_INS = ['x', 'adj', 'L0_gnn_weight', 'L0_gnn_bias']
_OUTS = [((4096, 64), 'float32')]


def kernel(**inputs):
    import numpy as _np
    import concourse.bacc as _bacc
    from concourse import mybir as _mybir
    from concourse.bass_utils import run_bass_kernel_spmd as _run

    nc = _bacc.Bacc("TRN2", target_bir_lowering=False, num_devices=1)
    arrays, args = {}, []
    for name in _INS:
        a = _np.ascontiguousarray(inputs[name])
        arrays[f"in_{name}_dram"] = a
        args.append(nc.dram_tensor(f"in_{name}_dram", a.shape, _mybir.dt.from_np(a.dtype), kind="ExternalInput").ap())
    for i, (shape, dtype) in enumerate(_OUTS):
        dt = _mybir.dt.from_np(_np.dtype(dtype))
        args.append(nc.dram_tensor(f"out_{i}_dram", shape, dt, kind="ExternalOutput").ap())
    gnn_decay_resnorm_kernel(nc, *args)
    r = _run(nc, [arrays], core_ids=[0])
    return r.results[0]["out_0_dram"]
```

```python
import concourse.bass as bass
from concourse import mybir
from contextlib import ExitStack


def gnn_decay_resnorm_kernel(nc: bass.Bass, x: bass.AP, adj: bass.AP, weight: bass.AP, bias: bass.AP, out: bass.AP):
    fp32, bf16, i16 = mybir.dt.float32, mybir.dt.bfloat16, mybir.dt.int16
    ALU = mybir.AluOpType
    ACT = mybir.ActivationFunctionType
    AX = mybir.AxisListType

    P = 128
    N, D = x.shape
    MAX_NEIGH = 100
    EPS = 1e-5
    LSB = 128
    REAL, CARRY, ONES = P - 2, P - 2, P - 1
    NB = -(-N // REAL)
    NBE = NB + NB % 2
    PAD = NBE * REAL
    TILES = N // P
    U = 4
    GROUPS = TILES // U
    BODY = 3
    CHUNK = [7, 7, 7, 6, 6]
    CH0 = [0, 7, 14, 21, 27]
    K = len(CHUNK)
    CW = max(CHUNK) * P
    BY_DVE = ()
    RING = 4
    LAG = 3
    ABOVE = -LSB
    TAG = 2 ** 14
    SELF = TAG - LSB
    SCALE = 2.0 ** (127 - MAX_NEIGH)
    ONE0 = LSB * (MAX_NEIGH + 1) - TAG - (ABOVE * (REAL - 1) + SELF + ABOVE)
    assert sum(CHUNK) == NB and ONE0 == -28 * LSB

    x_rows = x.rearrange("(p t) d -> p t d", p=P)
    out_rows = out.rearrange("(p t) d -> p t d", p=P)
    adj_rows = adj.rearrange("(p t) j -> p t j", p=P)
    QUARTER = TILES // 4
    HB = (NB - 1) // 2
    HALVES = [(0, HB), (HB, NBE)]
    NOW = 3

    ctx = ExitStack()
    with ctx:
        def sb(name, shape, dt):
            return ctx.enter_context(nc.sbuf_tensor(name, shape, dt))

        def pb(name, shape, dt):
            return ctx.enter_context(nc.psum_tensor(name, shape, dt))

        def sem(name):
            return ctx.enter_context(nc.semaphore(name))

        adj_sb = [sb(f"adj_sb{u}", [P, PAD], fp32) for u in range(U)]
        marks = [sb(f"marks{u}", [P, NBE, P], bf16) for u in range(U)]
        marksT = [sb(f"marksT{n}", [P, CW], bf16) for n in range(RING)]
        weights = [sb(f"weights{n}", [P, CW], i16) for n in range(RING)]
        h64 = sb("h64", [P, NB, 64], bf16)
        h32 = sb("h32", [P, NB, 32], bf16)
        h16 = sb("h16", [P, NB, 16], bf16)
        block_sum = sb("block_sum", [P, NB], fp32)
        c128 = sb("c128", [P, NB - 1], fp32)
        x_sb = sb("x_sb", [P, TILES, D], fp32)
        xT = sb("xT", [D, PAD], fp32)
        w_sb = sb("w_sb", [D, D], fp32)
        bias_sb = sb("bias_sb", [P, D], fp32)
        xb = sb("xb", [P, TILES, D], fp32)
        support = sb("support", [P, NBE, D], fp32)
        rest = sb("rest", [P, NBE, D], fp32)
        parts = sb("parts", [P, NBE, 3, D], bf16)
        ident_f = sb("ident_f", [P, P], fp32)
        ident = sb("ident", [P, P], bf16)
        rule_f = sb("rule_f", [P, P], fp32)
        rule = sb("rule", [P, P], bf16)
        z = sb("z", [P, U, D], fp32)
        zx = sb("zx", [P, U, D], fp32)
        stats = sb("stats", [P, U, 6], fp32)
        mv = sb("mv", [P, U, 2], fp32)
        veps = sb("veps", [P, U], fp32)
        rstd = sb("rstd", [P, U], fp32)
        mhalf = sb("mhalf", [P, U], fp32)
        eps = sb("eps", [P, U], fp32)
        zeros = sb("zeros", [P, NB], fp32)
        ones = sb("ones", [P, NB], fp32)
        y = sb("y", [P, 2, U, D], fp32)

        tr_ps = [pb(f"tr_ps{n}", [P, 1024], bf16) for n in range(2)]
        bits_ps = pb("bits_ps", [P, 2, 1024], fp32)
        sum_ps = [pb(f"sum_ps{n}", [P, 512], fp32) for n in range(2)]
        half_ps = bits_ps[:, :, :].rearrange("p a (b d) -> p a b d", d=D)
        xT_strided = xT[:, 0:N].rearrange("d (p t) -> d t p", t=TILES)
        sums = [sum_ps[n][:, 0:3 * D] for n in range(2)]

        adj_in = [sem(f"adj_in{u}") for u in range(U)]
        x_in, w_in, bias_in = sem("x_in"), sem("w_in"), sem("bias_in")
        out_done = [sem(f"out_done{n}") for n in range(2)]
        pool_step = sem("pool_step")
        ident_done = sem("ident_done")
        consts = sem("consts")
        parts_zero = sem("parts_zero")
        x_turned = sem("x_turned")
        xT_done = sem("xT_done")
        supported = sem("supported")
        support_out = sem("support_out")
        part_act = sem("part_act")
        part_dve = sem("part_dve")
        left = sem("left")
        reset = sem("reset")
        masked = sem("masked")
        halved = sem("halved")
        carried = sem("carried")
        transposed = sem("transposed")
        marksT_act, marksT_dve = sem("marksT_act"), sem("marksT_dve")
        counted = sem("counted")
        weighed = sem("weighed")
        multiplied = sem("multiplied")
        summed = sem("summed")
        added = sem("added")
        bn1, bn2 = sem("bn1"), sem("bn2")
        norm = sem("norm")
        HSTEPS, NSTEPS = 4, 4

        block = ctx.enter_context(nc.Block())

        CONSTS = 2 * U + 4

        def act_copies(k):
            return len([n for n in range(k) if n not in BY_DVE])

        def dve_copies(k):
            return k - act_copies(k)

        def wait_marksT(eng, g, u, k):
            t = g * U + u
            if k in BY_DVE:
                eng.wait_ge(marksT_dve, t * dve_copies(K) + dve_copies(k + 1))
            else:
                eng.wait_ge(marksT_act, t * act_copies(K) + act_copies(k + 1))

        def back(g, u, k, lag):
            s = u * K + k - lag
            return g + s // (U * K), s // K % U, s % K

        @block.sync
        def _(sp):
            def load(g, u, first):
                if not first:
                    sp.wait_ge(masked, 2 * ((g - 1) * U + u + 1))
                sp.dma_start(adj_sb[u][:, None, 0:N], adj_rows[:, bass.ds(g * U + u, 1), :]).then_inc(adj_in[u], 16)

            def store(g, half):
                sp.wait_ge(norm, NSTEPS * (g + 1))
                sp.dma_start(out_rows[:, bass.ds(g * U, U), :], y[:, half]).then_inc(out_done[half], 16)

            sp.dma_start(x_sb[:], x_rows).then_inc(x_in, 16)
            sp.dma_start(w_sb[:], weight).then_inc(w_in, 16)
            for u in range(U):
                load(0, u, True)
            sp.dma_start(bias_sb[:], bias.rearrange("(o d) -> o d", o=1).broadcast_to([P, D])).then_inc(bias_in, 16)
            for u in range(U):
                load(1, u, False)
            with sp.Fori(1, GROUPS // 2) as h:
                for i in range(2):
                    for u in range(U):
                        load(h * 2 + i, u, False)
                    store(h * 2 + i - 2, i)
            for i in range(2):
                store(GROUPS - 2 + i, i)
            for i in range(2):
                sp.wait_ge(out_done[i], 16 * GROUPS // 2)

        @block.gpsimd
        def _(pool):
            gp = nc.gpsimd
            n_step = [0]

            def step(ins):
                n_step[0] += 1
                ins.then_inc(pool_step, 1)

            def wait_steps():
                pool.wait_ge(pool_step, n_step[0])

            step(gp.memset(ident_f[:], 0.0))
            step(gp.iota(rule_f[:], pattern=[[-LSB, P]], base=ONE0, channel_multiplier=0,
                         allow_small_or_imprecise_dtypes=True))
            wait_steps()
            gp.affine_select(out=ident_f[:], in_=ident_f[:], compare_op=ALU.not_equal, fill=1.0, base=0,
                             pattern=[[-1, P]], channel_multiplier=1).then_inc(ident_done, 1)
            step(gp.affine_select(out=rule_f[:], in_=rule_f[:], compare_op=ALU.is_ge, fill=float(ABOVE), base=-ONES,
                                  pattern=[[0, P]], channel_multiplier=1))
            gp.memset(xT[:, N:PAD], 0.0).then_inc(consts, 1)
            gp.memset(support[:, NB:NBE, :], 0.0).then_inc(consts, 1)
            for u in range(U):
                gp.memset(adj_sb[u][:, N:PAD], 0.0).then_inc(consts, 1)
                gp.memset(marks[u][:, :, CARRY:P], 1.0).then_inc(consts, 1)
            gp.memset(c128[:], float(P)).then_inc(consts, 1)
            pool.wait_ge(ident_done, 1)
            gp.tensor_copy(ident[:], ident_f[:]).then_inc(ident_done, 1)
            wait_steps()
            step(gp.affine_select(out=rule_f[:], in_=rule_f[:], compare_op=ALU.is_gt, fill=0.0, base=0,
                                  pattern=[[-1, P]], channel_multiplier=1))
            wait_steps()
            step(gp.affine_select(out=rule_f[:], in_=rule_f[:], compare_op=ALU.not_equal, fill=float(SELF), base=0,
                                  pattern=[[-1, P]], channel_multiplier=1))
            wait_steps()
            step(gp.memset(rule_f[:, REAL:P], 0.0))
            wait_steps()
            gp.tensor_copy(rule[:], rule_f[:]).then_inc(consts, 1)
            step(gp.memset(mhalf[:], -0.5))
            step(gp.memset(eps[:], EPS))
            step(gp.memset(zeros[:], 0.0))
            step(gp.memset(ones[:], 1.0))
            pool.wait_ge(x_in, 16)
            pool.wait_ge(bias_in, 16)
            step(gp.tensor_tensor(xb[:], x_sb[:], bias_sb[:, None, :].broadcast_to([P, TILES, D]), ALU.add))
            wait_steps()

            def reset_carry(g, u):
                pool.wait_ge(transposed, K * (g * U + u + 1))
                gp.tensor_tensor(marks[u][:, 0:NB, CARRY], zeros[:], ones[:], ALU.add).then_inc(reset, 1)

            def add_x(g):
                pool.wait_ge(summed, U * (g + 1))
                gp.tensor_tensor(zx[:], z[:], xb[:, bass.ds(g * U, U), :], ALU.add).then_inc(added, 1)

            def normalise(g, half, stored):
                pool.wait_ge(bn2, U * (g + 1))
                gp.tensor_tensor(veps[:], mv[:, :, 1], eps[:], ALU.add).then_inc(norm, 1)
                pool.wait_ge(norm, NSTEPS * g + 1)
                gp.tensor_tensor(rstd[:], veps[:], mhalf[:], ALU.pow).then_inc(norm, 1)
                if stored is not None:
                    pool.wait_ge(out_done[half], 16 * stored)
                gp.tensor_tensor(y[:, half], zx[:], mv[:, :, 0:1].broadcast_to([P, U, D]),
                                 ALU.subtract).then_inc(norm, 1)
                pool.wait_ge(norm, NSTEPS * g + 3)
                gp.tensor_tensor(y[:, half], y[:, half], rstd[:, :, None].broadcast_to([P, U, D]),
                                 ALU.mult).then_inc(norm, 1)

            def group(g, half, stored):
                reset_carry(g, 0)
                add_x(g - 1)
                reset_carry(g, 1)
                normalise(g - 1, half, stored)
                reset_carry(g, 2)
                reset_carry(g, 3)

            for u in range(U):
                reset_carry(0, u)
            group(1, 0, None)
            group(2, 1, None)
            with pool.Fori(1, GROUPS // 2 - 1) as m:
                for half in range(2):
                    group(m * 2 + 1 + half, half, m)
            add_x(GROUPS - 2)
            normalise(GROUPS - 2, 0, GROUPS // 2 - 1)
            add_x(GROUPS - 1)
            normalise(GROUPS - 1, 1, GROUPS // 2 - 1)

        @block.tensor
        def _(pe):
            mm = nc.tensor.matmul
            pe.wait_ge(ident_done, 1)
            pe.wait_ge(x_in, 16)
            for q in range(4):
                if q >= 2:
                    pe.wait_ge(xT_done, q - 1)
                for n in range(QUARTER):
                    last = nc.tensor.transpose(bits_ps[0:D, q % 2, n * P:(n + 1) * P], x_sb[:, q * QUARTER + n, :],
                                               ident_f[:])
                last.then_inc(x_turned, 1)
            pe.wait_ge(w_in, 16)
            pe.wait_ge(xT_done, 4)
            pe.wait_ge(consts, 1)
            for h, (lo, hi) in enumerate(HALVES):
                for b in range(lo, min(hi, NB)):
                    dst = half_ps[0:REAL, h, b - lo] if b < NB - 1 else sum_ps[0][0:REAL, 0:D]
                    last = mm(dst, xT[:, b * REAL:(b + 1) * REAL], w_sb[:], start=True, stop=True)
                last.then_inc(supported, 1)
            pe.wait_ge(ident_done, 2)
            pe.wait_ge(consts, CONSTS)

            def transposes(g, u, k, first):
                if k == 0:
                    pe.wait_ge(carried, g * U + u + 1)
                s = u * K + k
                if s >= 2 or not first:
                    wait_marksT(pe, *back(g, u, k, 2))
                for n in range(CHUNK[k]):
                    last = nc.tensor.transpose(tr_ps[s % 2][:, n * P:(n + 1) * P],
                                               marks[u][:, CH0[k] + n, :], ident[:])
                last.then_inc(transposed, 1)

            def count(g, u, k, first):
                s = u * K + k
                wait_marksT(pe, g, u, k)
                if s >= 2 or not first:
                    pe.wait_ge(weighed, g * (U * K) + s - 1)
                else:
                    pe.wait_ge(support_out, 1 + 2 * s)
                for c in range(0, CHUNK[k] * P, 512):
                    e = min(c + 512, CHUNK[k] * P)
                    last = mm(bits_ps[:, s % 2, c:e], rule[:], marksT[s % RING][:, c:e], start=True, stop=True)
                last.then_inc(counted, 1)

            def product(g, u, k, first):
                s = u * K + k
                pe.wait_ge(weighed, g * (U * K) + s + 1)
                if k == 0:
                    if u >= 2 or not first:
                        pe.wait_ge(summed, g * U + u - 1)
                if first and u == 0:
                    pe.wait_ge(part_act, 3)
                    if CH0[k] + CHUNK[k] > HB:
                        pe.wait_ge(part_act, 4)
                        pe.wait_ge(part_dve, 2)
                    pe.wait_ge(parts_zero, 1)
                w = weights[s % RING][:].bitcast(bf16)
                for n in range(CHUNK[k]):
                    b = CH0[k] + n
                    last = mm(sums[u % 2], w[:, n * P:(n + 1) * P], parts[:, b].rearrange("p a d -> p (a d)"),
                              start=(b == 0), stop=(b == NB - 1))
                last.then_inc(multiplied, 1)

            def group(g, first):
                for u in range(U):
                    for k in range(K):
                        s = u * K + k
                        transposes(g, u, k, first)
                        for fn, lag in ((count, 1), (product, LAG)):
                            if s >= lag or not first:
                                fn(*back(g, u, k, lag), first and s >= lag)

            group(0, True)
            with pe.Fori(1, GROUPS - 1, BODY) as g:
                for i in range(BODY):
                    group(g + i, False)
            group(GROUPS - 1, False)
            for d in range(LAG):
                if d < 1:
                    count(GROUPS - 1, U - 1, K - 1, False)
                product(*back(GROUPS - 1, U - 1, K - 1, LAG - 1 - d), False)

        @block.scalar
        def _(act):
            for q in range(4):
                act.wait_ge(x_turned, q + 1)
                nc.scalar.copy(xT_strided[:, q * QUARTER:(q + 1) * QUARTER, :],
                               bits_ps[0:D, q % 2, :].rearrange("d (t p) -> d t p", p=P)).then_inc(xT_done, 1)

            def part(h, n, src):
                lo, hi = HALVES[h]
                nc.scalar.copy(parts[0:REAL, lo:hi, n, :], src[0:REAL, lo:hi, :]).then_inc(part_act, 1)

            act.wait_ge(supported, 1)
            nc.scalar.mul(support[0:REAL, 0:HB, :], half_ps[0:REAL, 0], SCALE).then_inc(support_out, 1)
            act.wait_ge(support_out, 1)
            act.wait_ge(parts_zero, 1)
            part(0, 0, support)
            for n in (1, 2):
                act.wait_ge(left, n)
                part(0, n, rest)
            act.wait_ge(supported, 2)
            nc.scalar.mul(support[0:REAL, HB:2 * HB, :], half_ps[0:REAL, 1], SCALE).then_inc(support_out, 1)
            nc.scalar.mul(support[0:REAL, NB - 1, :], sum_ps[0][0:REAL, 0:D], SCALE).then_inc(support_out, 1)
            act.wait_ge(support_out, 3)
            act.wait_ge(consts, 2)
            part(1, 0, support)

            def copy_marks(g, u, k, first):
                s = u * K + k
                act.wait_ge(transposed, g * (U * K) + s + 1)
                if s >= RING or not first:
                    act.wait_ge(counted, g * (U * K) + s + 1 - RING)
                c = CHUNK[k] * P
                nc.scalar.copy(marksT[s % RING][:, 0:c].bitcast(fp32),
                               tr_ps[s % 2][:, 0:c].bitcast(fp32)).then_inc(marksT_act, 1)

            def weigh(g, u, k, first):
                s = u * K + k
                act.wait_ge(counted, g * (U * K) + s + 1)
                if s >= RING or not first:
                    act.wait_ge(multiplied, g * (U * K) + s + 1 - RING)
                c = CHUNK[k] * P
                nc.scalar.activation(weights[s % RING][:, 0:c], bits_ps[:, s % 2, 0:c],
                                     ACT.Relu).then_inc(weighed, 1)

            def group(g, first):
                for u in range(U):
                    for k in range(K):
                        if k not in BY_DVE:
                            copy_marks(g, u, k, first)
                        s = u * K + k
                        if s >= 1 or not first:
                            weigh(*back(g, u, k, 1), first and s >= 1)

            group(0, True)
            with act.Fori(1, GROUPS - 1, BODY) as g:
                for i in range(BODY):
                    group(g + i, False)
            group(GROUPS - 1, False)
            weigh(GROUPS - 1, U - 1, K - 1, False)

        @block.vector
        def _(dve):
            v = nc.vector
            MARK_HALVES = [(0, NB // 2), (NB // 2, NBE)]

            def leave(h, n):
                lo, hi = HALVES[h]
                if h == 0 or n == 0:
                    dve.wait_ge(part_act, 3 * h + n + 1)
                else:
                    dve.wait_ge(part_dve, 1)
                    dve.wait_ge(left, 3)
                src = rest if n else support
                v.tensor_tensor(rest[0:REAL, lo:hi, :], src[0:REAL, lo:hi, :], parts[0:REAL, lo:hi, n, :],
                                ALU.subtract).then_inc(left, 1)

            def part(n):
                dve.wait_ge(left, 2 + n)
                v.tensor_copy(parts[0:REAL, HB:NBE, n, :], rest[0:REAL, HB:NBE, :]).then_inc(part_dve, 1)

            def mark(g, u, half, first):
                lo, hi = MARK_HALVES[half]
                if half == 0:
                    dve.wait_ge(adj_in[u], 16 * (g + 1))
                    if not first:
                        dve.wait_ge(reset, (g - 1) * U + u + 1)
                v.tensor_scalar(marks[u][:, lo:hi, 0:REAL],
                                adj_sb[u][:, lo * REAL:hi * REAL].rearrange("p (b c) -> p b c", c=REAL),
                                0.0, 1.0, ALU.not_equal, ALU.add).then_inc(masked, 1)

            def halve(g, u, n):
                t = g * U + u
                if n == 0:
                    dve.wait_ge(masked, 2 * t + 2)
                else:
                    dve.wait_ge(halved, HSTEPS * t + n)
                src, dst, w = (marks[u], h64, h32)[n], (h64, h32, h16)[n], 64 >> n
                v.tensor_tensor(dst[:, :, :], src[:, 0:NB, 0:w], src[:, 0:NB, w:2 * w], ALU.add).then_inc(halved, 1)

            def sum_blocks(g, u):
                dve.wait_ge(halved, HSTEPS * (g * U + u) + 3)
                v.tensor_reduce(block_sum[:], h16[:, :, :], AX.X, ALU.add).then_inc(halved, 1)

            def carry(g, u):
                dve.wait_ge(halved, HSTEPS * (g * U + u) + 4)
                v.tensor_tensor_scan(marks[u][:, NB - 2::-1, CARRY], block_sum[:, NB - 1:0:-1], c128[:],
                                     1.0, ALU.add, ALU.subtract).then_inc(carried, 1)

            def copy_marks(g, u, k, first):
                s = u * K + k
                dve.wait_ge(transposed, g * (U * K) + s + 1)
                if s >= RING or not first:
                    dve.wait_ge(counted, g * (U * K) + s + 1 - RING)
                c = CHUNK[k] * P
                v.tensor_copy(marksT[s % RING][:, 0:c].bitcast(fp32),
                              tr_ps[s % 2][:, 0:c].bitcast(fp32)).then_inc(marksT_dve, 1)

            def add_parts(g, u, first):
                dve.wait_ge(multiplied, K * (g * U + u + 1))
                if u == 0 and not first:
                    dve.wait_ge(added, g)
                v.tensor_reduce(z[:, u, :], sums[u % 2].rearrange("p (a d) -> p d a", a=3), AX.X,
                                ALU.add).then_inc(summed, 1)

            def statistics(g):
                dve.wait_ge(added, g + 1)
                for u in range(U):
                    v.bn_stats(stats[:, u, :], zx[:, u, :]).then_inc(bn1, 1)

            def wait_statistics(g):
                dve.wait_ge(bn1, U * (g + 1))

            def aggregate():
                for u in range(U):
                    v.bn_aggr(mv[:, u, :], stats[:, u, :]).then_inc(bn2, 1)

            def before(g, u, lag):
                return (g, u - lag) if u >= lag else (g - 1, u - lag + U)

            def tile(g, u, first):
                last = before(g, u, 1)
                put_off = not (first and u <= NOW)
                mark(g, u, 0, first)
                if first and u == 1:
                    leave(0, 1)
                if not (first and u < 3):
                    add_parts(*before(g, u, 3), first)
                if put_off:
                    sum_blocks(*last)
                mark(g, u, 1, first)
                if put_off:
                    carry(*last)
                if u == 3 and not first:
                    statistics(g - 1)
                halve(g, u, 0)
                if u == 3 and not first:
                    wait_statistics(g - 1)
                halve(g, u, 1)
                if u == 3 and not first:
                    aggregate()
                halve(g, u, 2)
                if first and u < NOW:
                    sum_blocks(g, u)
                    carry(g, u)

            v.memset(parts[96:P], 0.0).then_inc(parts_zero, 1)
            dve.wait_ge(consts, CONSTS - 1)
            tile(0, 0, True)
            leave(0, 0)
            tile(0, 1, True)
            leave(1, 0)
            part(1)
            leave(1, 1)
            part(2)
            for u in range(2, U):
                tile(0, u, True)
            with dve.Fori(1, GROUPS - 1, BODY) as g:
                for i in range(BODY):
                    for u in range(U):
                        tile(g + i, u, False)
            G = GROUPS - 1
            for u in range(U):
                tile(G, u, False)
            sum_blocks(G, U - 1)
            carry(G, U - 1)
            add_parts(G, U - 3, False)
            add_parts(G, U - 2, False)
            add_parts(G, U - 1, False)
            statistics(G)
            wait_statistics(G)
            aggregate()


_INS = ['x', 'adj', 'L0_gnn_weight', 'L0_gnn_bias']
_OUTS = [((4096, 64), 'float32')]


def kernel(**inputs):
    import numpy as _np
    import concourse.bacc as _bacc
    from concourse import mybir as _mybir
    from concourse.bass_utils import run_bass_kernel_spmd as _run

    nc = _bacc.Bacc("TRN2", target_bir_lowering=False, num_devices=1)
    arrays, args = {}, []
    for name in _INS:
        a = _np.ascontiguousarray(inputs[name])
        arrays[f"in_{name}_dram"] = a
        args.append(nc.dram_tensor(f"in_{name}_dram", a.shape, _mybir.dt.from_np(a.dtype), kind="ExternalInput").ap())
    for i, (shape, dtype) in enumerate(_OUTS):
        dt = _mybir.dt.from_np(_np.dtype(dtype))
        args.append(nc.dram_tensor(f"out_{i}_dram", shape, dt, kind="ExternalOutput").ap())
    gnn_decay_resnorm_kernel(nc, *args)
    r = _run(nc, [arrays], core_ids=[0])
    return r.results[0]["out_0_dram"]
```

```python
import concourse.bass as bass
from concourse import mybir
from contextlib import ExitStack


def gnn_decay_resnorm_kernel(nc: bass.Bass, x: bass.AP, adj: bass.AP, weight: bass.AP, bias: bass.AP, out: bass.AP):
    fp32, bf16, i16 = mybir.dt.float32, mybir.dt.bfloat16, mybir.dt.int16
    ALU = mybir.AluOpType
    ACT = mybir.ActivationFunctionType
    AX = mybir.AxisListType

    P = 128
    N, D = x.shape
    MAX_NEIGH = 100
    EPS = 1e-5
    LSB = 128
    REAL, CARRY, ONES = P - 2, P - 2, P - 1
    NB = -(-N // REAL)
    NBE = NB + NB % 2
    PAD = NBE * REAL
    TILES = N // P
    U = 4
    GROUPS = TILES // U
    BODY = 3
    CHUNK = [7, 7, 7, 6, 6]
    CH0 = [0, 7, 14, 21, 27]
    K = len(CHUNK)
    CW = max(CHUNK) * P
    RING = 4
    LAG = 2
    ABOVE = -LSB
    TAG = 2 ** 14
    SELF = TAG - LSB
    SCALE = 2.0 ** (127 - MAX_NEIGH)
    ONE0 = LSB * (MAX_NEIGH + 1) - TAG - (ABOVE * (REAL - 1) + SELF + ABOVE)
    assert sum(CHUNK) == NB and ONE0 == -28 * LSB

    x_rows = x.rearrange("(p t) d -> p t d", p=P)
    out_rows = out.rearrange("(p t) d -> p t d", p=P)
    adj_rows = adj.rearrange("(p t) j -> p t j", p=P)
    QUARTER = TILES // 4
    HB = (NB - 1) // 2
    HALVES = [(0, HB), (HB, NB)]
    WARM_UP = 16
    NOW = 3

    ctx = ExitStack()
    with ctx:
        def sb(name, shape, dt):
            return ctx.enter_context(nc.sbuf_tensor(name, shape, dt))

        def pb(name, shape, dt):
            return ctx.enter_context(nc.psum_tensor(name, shape, dt))

        def sem(name):
            return ctx.enter_context(nc.semaphore(name))

        adj_sb = [sb(f"adj_sb{u}", [P, PAD], fp32) for u in range(U)]
        marks = [sb(f"marks{u}", [P, NBE, P], bf16) for u in range(U)]
        marksT = [sb(f"marksT{n}", [P, CW], bf16) for n in range(RING)]
        weights = [sb(f"weights{n}", [P, CW], i16) for n in range(RING)]
        h64 = sb("h64", [P, NB, 64], bf16)
        h32 = sb("h32", [P, NB, 32], bf16)
        h16 = sb("h16", [P, NB, 16], bf16)
        block_sum = sb("block_sum", [P, NB], fp32)
        c128 = sb("c128", [P, NB - 1], fp32)
        x_sb = sb("x_sb", [P, TILES, D], fp32)
        xT = sb("xT", [D, PAD], fp32)
        w_sb = sb("w_sb", [D, D], fp32)
        bias_sb = sb("bias_sb", [P, D], fp32)
        xb = sb("xb", [P, TILES, D], fp32)
        support = sb("support", [P, NBE, D], fp32)
        rest = sb("rest", [P, NBE, D], fp32)
        parts = sb("parts", [P, NBE, 3, D], bf16)
        ident_f = sb("ident_f", [P, P], fp32)
        ident = sb("ident", [P, P], bf16)
        rule_f = sb("rule_f", [P, P], fp32)
        rule = sb("rule", [P, P], bf16)
        z = sb("z", [P, U, D], fp32)
        zx = sb("zx", [P, U, D], fp32)
        stats = sb("stats", [P, U, 6], fp32)
        mv = sb("mv", [P, U, 2], fp32)
        veps = sb("veps", [P, U], fp32)
        rstd = sb("rstd", [P, U], fp32)
        mhalf = sb("mhalf", [P, U], fp32)
        eps = sb("eps", [P, U], fp32)
        zeros = sb("zeros", [P, NB], fp32)
        ones = sb("ones", [P, NB], fp32)
        y = sb("y", [P, 2, U, D], fp32)

        tr_ps = [pb(f"tr_ps{n}", [P, 1024], bf16) for n in range(2)]
        bits_ps = pb("bits_ps", [P, 2, 1024], fp32)
        sum_ps = [pb(f"sum_ps{n}", [P, 512], fp32) for n in range(2)]
        half_ps = bits_ps[:, :, :].rearrange("p a (b d) -> p a b d", d=D)
        xT_strided = xT[:, 0:N].rearrange("d (p t) -> d t p", t=TILES)
        sums = [sum_ps[n][:, 0:3 * D] for n in range(2)]

        adj_in = [sem(f"adj_in{u}") for u in range(U)]
        x_in = [sem(f"x_in{q}") for q in range(4)]
        w_in, bias_in = sem("w_in"), sem("bias_in")
        out_done = [sem(f"out_done{n}") for n in range(2)]
        pool_step = sem("pool_step")
        ident_done = sem("ident_done")
        consts = sem("consts")
        parts_zero = sem("parts_zero")
        x_turned = sem("x_turned")
        xT_done = sem("xT_done")
        supported = sem("supported")
        support_out = sem("support_out")
        part = sem("part")
        left = sem("left")
        split = sem("split")
        reset = sem("reset")
        masked = sem("masked")
        halved = sem("halved")
        carried = sem("carried")
        transposed = sem("transposed")
        copied = sem("copied")
        counted = sem("counted")
        weighed = sem("weighed")
        multiplied = sem("multiplied")
        summed = sem("summed")
        added = sem("added")
        bn1, bn2 = sem("bn1"), sem("bn2")
        norm = sem("norm")
        xb_done = sem("xb_done")
        tail = sem("tail")
        tail_pool = sem("tail_pool")
        HSTEPS, NSTEPS, SPLITS = 4, 4, 5

        block = ctx.enter_context(nc.Block())

        CONSTS = 2 * U + 4

        def back(g, u, k, lag):
            s = u * K + k - lag
            return g + s // (U * K), s // K % U, s % K

        @block.sync
        def _(sp):
            def load(g, u, first):
                if not first:
                    sp.wait_ge(masked, 2 * ((g - 1) * U + u + 1))
                sp.dma_start(adj_sb[u][:, None, 0:N], adj_rows[:, bass.ds(g * U + u, 1), :]).then_inc(adj_in[u], 16)

            def store(g, half):
                sp.wait_ge(norm, NSTEPS * (g + 1))
                sp.dma_start(out_rows[:, bass.ds(g * U, U), :], y[:, half]).then_inc(out_done[half], 16)

            for q in range(4):
                rows = slice(q * QUARTER, (q + 1) * QUARTER)
                sp.dma_start(x_sb[:, rows, :], x_rows[:, rows, :]).then_inc(x_in[q], 16)
            sp.dma_start(w_sb[:], weight).then_inc(w_in, 16)
            for u in range(U):
                load(0, u, True)
            sp.dma_start(bias_sb[:], bias.rearrange("(o d) -> o d", o=1).broadcast_to([P, D])).then_inc(bias_in, 16)
            for u in range(U):
                load(1, u, False)
            with sp.Fori(1, GROUPS // 2) as h:
                for i in range(2):
                    for u in range(U):
                        load(h * 2 + i, u, False)
                    store(h * 2 + i - 2, i)
            store(GROUPS - 2, 0)
            sp.wait_ge(tail, 4 * U)
            sp.dma_start(out_rows[:, TILES - U:TILES, :], y[:, 1]).then_inc(out_done[1], 16)
            for i in range(2):
                sp.wait_ge(out_done[i], 16 * GROUPS // 2)

        @block.gpsimd
        def _(pool):
            gp = nc.gpsimd
            n_step = [0]

            def step(ins):
                n_step[0] += 1
                ins.then_inc(pool_step, 1)

            def wait_steps():
                pool.wait_ge(pool_step, n_step[0])

            step(gp.memset(ident_f[:], 0.0))
            step(gp.iota(rule_f[:], pattern=[[-LSB, P]], base=ONE0, channel_multiplier=0,
                         allow_small_or_imprecise_dtypes=True))
            wait_steps()
            gp.affine_select(out=ident_f[:], in_=ident_f[:], compare_op=ALU.not_equal, fill=1.0, base=0,
                             pattern=[[-1, P]], channel_multiplier=1).then_inc(ident_done, 1)
            step(gp.affine_select(out=rule_f[:], in_=rule_f[:], compare_op=ALU.is_ge, fill=float(ABOVE), base=-ONES,
                                  pattern=[[0, P]], channel_multiplier=1))
            gp.memset(xT[:, N:PAD], 0.0).then_inc(consts, 1)
            gp.memset(support[:, NB:NBE, :], 0.0).then_inc(consts, 1)
            for u in range(U):
                gp.memset(adj_sb[u][:, N:PAD], 0.0).then_inc(consts, 1)
                gp.memset(marks[u][:, :, CARRY:P], 1.0).then_inc(consts, 1)
            gp.memset(c128[:], float(P)).then_inc(consts, 1)
            pool.wait_ge(ident_done, 1)
            gp.tensor_copy(ident[:], ident_f[:]).then_inc(ident_done, 1)
            wait_steps()
            step(gp.affine_select(out=rule_f[:], in_=rule_f[:], compare_op=ALU.is_gt, fill=0.0, base=0,
                                  pattern=[[-1, P]], channel_multiplier=1))
            wait_steps()
            step(gp.affine_select(out=rule_f[:], in_=rule_f[:], compare_op=ALU.not_equal, fill=float(SELF), base=0,
                                  pattern=[[-1, P]], channel_multiplier=1))
            wait_steps()
            step(gp.memset(rule_f[:, REAL:P], 0.0))
            wait_steps()
            gp.tensor_copy(rule[:], rule_f[:]).then_inc(consts, 1)
            step(gp.memset(mhalf[:], -0.5))
            step(gp.memset(eps[:], EPS))
            step(gp.memset(zeros[:], 0.0))
            step(gp.memset(ones[:], 1.0))
            for n, src in enumerate((support, rest)):
                pool.wait_ge(part, n + 1)
                gp.tensor_tensor(rest[0:REAL, 0:HB, :], src[0:REAL, 0:HB, :], parts[0:REAL, 0:HB, n, :],
                                 ALU.subtract).then_inc(left, 1)
            for q in range(4):
                pool.wait_ge(x_in[q], 16)
            pool.wait_ge(bias_in, 16)
            gp.tensor_tensor(xb[:], x_sb[:], bias_sb[:, None, :].broadcast_to([P, TILES, D]),
                             ALU.add).then_inc(xb_done, 1)
            wait_steps()
            pool.wait_ge(xb_done, 1)

            def reset_carry(g, u):
                pool.wait_ge(transposed, K * (g * U + u + 1))
                gp.tensor_tensor(marks[u][:, 0:NB, CARRY], zeros[:], ones[:], ALU.add).then_inc(reset, 1)

            def add_x(g):
                pool.wait_ge(summed, U * (g + 1))
                gp.tensor_tensor(zx[:], z[:], xb[:, bass.ds(g * U, U), :], ALU.add).then_inc(added, 1)

            def normalise(g, half, stored):
                pool.wait_ge(bn2, U * (g + 1))
                gp.tensor_tensor(veps[:], mv[:, :, 1], eps[:], ALU.add).then_inc(norm, 1)
                pool.wait_ge(norm, NSTEPS * g + 1)
                gp.tensor_tensor(rstd[:], veps[:], mhalf[:], ALU.pow).then_inc(norm, 1)
                if stored is not None:
                    pool.wait_ge(out_done[half], 16 * stored)
                gp.tensor_tensor(y[:, half], zx[:], mv[:, :, 0:1].broadcast_to([P, U, D]),
                                 ALU.subtract).then_inc(norm, 1)
                pool.wait_ge(norm, NSTEPS * g + 3)
                gp.tensor_tensor(y[:, half], y[:, half], rstd[:, :, None].broadcast_to([P, U, D]),
                                 ALU.mult).then_inc(norm, 1)

            def group(g, half, stored):
                reset_carry(g, 0)
                add_x(g - 1)
                reset_carry(g, 1)
                normalise(g - 1, half, stored)
                reset_carry(g, 2)
                reset_carry(g, 3)

            for u in range(U):
                reset_carry(0, u)
            group(1, 0, None)
            group(2, 1, None)
            with pool.Fori(1, GROUPS // 2 - 1) as m:
                for half in range(2):
                    group(m * 2 + 1 + half, half, m)
            add_x(GROUPS - 2)
            normalise(GROUPS - 2, 0, GROUPS // 2 - 1)
            for u in range(U):
                pool.wait_ge(tail, 4 * u + 3)
                gp.tensor_tensor(veps[:, u:u + 1], mv[:, u, 1:2], eps[:, 0:1], ALU.add).then_inc(tail_pool, 1)
                pool.wait_ge(tail_pool, 2 * u + 1)
                gp.tensor_tensor(rstd[:, u:u + 1], veps[:, u:u + 1], mhalf[:, 0:1], ALU.pow).then_inc(tail_pool, 1)

        @block.tensor
        def _(pe):
            mm = nc.tensor.matmul
            pe.wait_ge(ident_done, 1)
            for n in range(WARM_UP):
                nc.tensor.transpose(sum_ps[1][:, 0:P], ident_f[:], ident_f[:])
            for q in range(4):
                pe.wait_ge(x_in[q], 16)
                if q >= 2:
                    pe.wait_ge(xT_done, q - 1)
                for n in range(QUARTER):
                    last = nc.tensor.transpose(bits_ps[0:D, q % 2, n * P:(n + 1) * P], x_sb[:, q * QUARTER + n, :],
                                               ident_f[:])
                last.then_inc(x_turned, 1)
            pe.wait_ge(w_in, 16)
            pe.wait_ge(xT_done, 4)
            pe.wait_ge(consts, 1)
            for h, (lo, hi) in enumerate(HALVES):
                for b in range(lo, hi):
                    dst = half_ps[0:REAL, h, b - lo] if b < NB - 1 else sum_ps[0][0:REAL, 0:D]
                    last = mm(dst, xT[:, b * REAL:(b + 1) * REAL], w_sb[:], start=True, stop=True)
                last.then_inc(supported, 1)
            pe.wait_ge(ident_done, 2)
            pe.wait_ge(consts, CONSTS)

            def transposes(g, u, k, first):
                if k == 0:
                    pe.wait_ge(carried, g * U + u + 1)
                s = u * K + k
                if s >= 2 or not first:
                    pe.wait_ge(copied, g * (U * K) + s - 1)
                for n in range(CHUNK[k]):
                    last = nc.tensor.transpose(tr_ps[s % 2][:, n * P:(n + 1) * P],
                                               marks[u][:, CH0[k] + n, :], ident[:])
                last.then_inc(transposed, 1)

            def count(g, u, k, first):
                s = u * K + k
                pe.wait_ge(copied, g * (U * K) + s + 1)
                if s >= 2 or not first:
                    pe.wait_ge(weighed, g * (U * K) + s - 1)
                else:
                    pe.wait_ge(support_out, 1 + 2 * s)
                for c in range(0, CHUNK[k] * P, 512):
                    e = min(c + 512, CHUNK[k] * P)
                    last = mm(bits_ps[:, s % 2, c:e], rule[:], marksT[s % RING][:, c:e], start=True, stop=True)
                last.then_inc(counted, 1)

            def product(g, u, k, first):
                s = u * K + k
                pe.wait_ge(weighed, g * (U * K) + s + 1)
                if k == 0:
                    if u >= 2 or not first:
                        pe.wait_ge(summed, g * U + u - 1)
                if first and u == 0:
                    pe.wait_ge(part, 3)
                    if CH0[k] + CHUNK[k] > HB:
                        pe.wait_ge(split, SPLITS)
                    pe.wait_ge(parts_zero, 1)
                w = weights[s % RING][:].bitcast(bf16)
                for n in range(CHUNK[k]):
                    b = CH0[k] + n
                    last = mm(sums[u % 2], w[:, n * P:(n + 1) * P], parts[:, b].rearrange("p a d -> p (a d)"),
                              start=(b == 0), stop=(b == NB - 1))
                last.then_inc(multiplied, 1)

            def group(g, first):
                for u in range(U):
                    for k in range(K):
                        s = u * K + k
                        transposes(g, u, k, first)
                        for fn, lag in ((count, 1), (product, LAG)):
                            if s >= lag or not first:
                                fn(*back(g, u, k, lag), first and s >= lag)

            group(0, True)
            with pe.Fori(1, GROUPS - 1, BODY) as g:
                for i in range(BODY):
                    group(g + i, False)
            group(GROUPS - 1, False)
            for d in range(LAG):
                if d < 1:
                    count(GROUPS - 1, U - 1, K - 1, False)
                product(*back(GROUPS - 1, U - 1, K - 1, LAG - 1 - d), False)

        @block.scalar
        def _(act):
            for q in range(4):
                act.wait_ge(x_turned, q + 1)
                nc.scalar.copy(xT_strided[:, q * QUARTER:(q + 1) * QUARTER, :],
                               bits_ps[0:D, q % 2, :].rearrange("d (t p) -> d t p", p=P)).then_inc(xT_done, 1)

            act.wait_ge(supported, 1)
            nc.scalar.mul(support[0:REAL, 0:HB, :], half_ps[0:REAL, 0], SCALE).then_inc(support_out, 1)
            act.wait_ge(support_out, 1)
            act.wait_ge(parts_zero, 1)

            def first_half(n, src):
                if n:
                    act.wait_ge(left, n)
                nc.scalar.copy(parts[0:REAL, 0:HB, n, :], src[0:REAL, 0:HB, :]).then_inc(part, 1)

            first_half(0, support)
            first_half(1, rest)
            act.wait_ge(supported, 2)
            nc.scalar.mul(support[0:REAL, HB:2 * HB, :], half_ps[0:REAL, 1], SCALE).then_inc(support_out, 1)
            nc.scalar.mul(support[0:REAL, NB - 1, :], sum_ps[0][0:REAL, 0:D], SCALE).then_inc(support_out, 1)

            def copy_marks(g, u, k, first):
                s = u * K + k
                act.wait_ge(transposed, g * (U * K) + s + 1)
                if s >= RING or not first:
                    act.wait_ge(counted, g * (U * K) + s + 1 - RING)
                c = CHUNK[k] * P
                nc.scalar.copy(marksT[s % RING][:, 0:c].bitcast(fp32),
                               tr_ps[s % 2][:, 0:c].bitcast(fp32)).then_inc(copied, 1)

            def weigh(g, u, k, first):
                s = u * K + k
                act.wait_ge(counted, g * (U * K) + s + 1)
                if s >= RING or not first:
                    act.wait_ge(multiplied, g * (U * K) + s + 1 - RING)
                c = CHUNK[k] * P
                nc.scalar.activation(weights[s % RING][:, 0:c], bits_ps[:, s % 2, 0:c],
                                     ACT.Relu).then_inc(weighed, 1)

            def group(g, first):
                for u in range(U):
                    for k in range(K):
                        if first and u * K + k == 1:
                            first_half(2, rest)
                        copy_marks(g, u, k, first)
                        s = u * K + k
                        if s >= 1 or not first:
                            weigh(*back(g, u, k, 1), first and s >= 1)

            group(0, True)
            with act.Fori(1, GROUPS - 1, BODY) as g:
                for i in range(BODY):
                    group(g + i, False)
            group(GROUPS - 1, False)
            weigh(GROUPS - 1, U - 1, K - 1, False)

        @block.vector
        def _(dve):
            v = nc.vector
            MARK_HALVES = [(0, NB // 2), (NB // 2, NBE)]

            def split_second_half():
                src = support[0:REAL, HB:NBE, :]
                left = rest[0:REAL, HB:NBE, :]
                dve.wait_ge(support_out, 3)
                for n in range(3):
                    if n:
                        dve.wait_ge(split, 2 * n)
                    v.tensor_copy(parts[0:REAL, HB:NBE, n, :], src).then_inc(split, 1)
                    if n < 2:
                        dve.wait_ge(split, 2 * n + 1)
                        v.tensor_tensor(left, src, parts[0:REAL, HB:NBE, n, :], ALU.subtract).then_inc(split, 1)
                        src = left

            def mark(g, u, half, first):
                lo, hi = MARK_HALVES[half]
                if half == 0:
                    dve.wait_ge(adj_in[u], 16 * (g + 1))
                    if not first:
                        dve.wait_ge(reset, (g - 1) * U + u + 1)
                v.tensor_scalar(marks[u][:, lo:hi, 0:REAL],
                                adj_sb[u][:, lo * REAL:hi * REAL].rearrange("p (b c) -> p b c", c=REAL),
                                0.0, 1.0, ALU.not_equal, ALU.add).then_inc(masked, 1)

            def halve(g, u, n):
                t = g * U + u
                if n == 0:
                    dve.wait_ge(masked, 2 * t + 2)
                else:
                    dve.wait_ge(halved, HSTEPS * t + n)
                src, dst, w = (marks[u], h64, h32)[n], (h64, h32, h16)[n], 64 >> n
                v.tensor_tensor(dst[:, :, :], src[:, 0:NB, 0:w], src[:, 0:NB, w:2 * w], ALU.add).then_inc(halved, 1)

            def sum_blocks(g, u):
                dve.wait_ge(halved, HSTEPS * (g * U + u) + 3)
                v.tensor_reduce(block_sum[:], h16[:, :, :], AX.X, ALU.add).then_inc(halved, 1)

            def carry(g, u):
                dve.wait_ge(halved, HSTEPS * (g * U + u) + 4)
                v.tensor_tensor_scan(marks[u][:, NB - 2::-1, CARRY], block_sum[:, NB - 1:0:-1], c128[:],
                                     1.0, ALU.add, ALU.subtract).then_inc(carried, 1)

            def add_parts(g, u, first):
                dve.wait_ge(multiplied, K * (g * U + u + 1))
                if u == 0 and not first:
                    dve.wait_ge(added, g)
                v.tensor_reduce(z[:, u, :], sums[u % 2].rearrange("p (a d) -> p d a", a=3), AX.X,
                                ALU.add).then_inc(summed, 1)

            def statistics(g):
                dve.wait_ge(added, g + 1)
                for u in range(U):
                    v.bn_stats(stats[:, u, :], zx[:, u, :]).then_inc(bn1, 1)

            def wait_statistics(g):
                dve.wait_ge(bn1, U * (g + 1))

            def aggregate():
                for u in range(U):
                    v.bn_aggr(mv[:, u, :], stats[:, u, :]).then_inc(bn2, 1)

            def before(g, u, lag):
                return (g, u - lag) if u >= lag else (g - 1, u - lag + U)

            def tile(g, u, first):
                last = before(g, u, 1)
                put_off = not (first and u <= NOW)
                mark(g, u, 0, first)
                if not (first and u < 3):
                    add_parts(*before(g, u, 3), first)
                if put_off:
                    sum_blocks(*last)
                mark(g, u, 1, first)
                if put_off:
                    carry(*last)
                if u == 3 and not first:
                    statistics(g - 1)
                if first and u == 2:
                    split_second_half()
                halve(g, u, 0)
                if u == 3 and not first:
                    wait_statistics(g - 1)
                halve(g, u, 1)
                if u == 3 and not first:
                    aggregate()
                halve(g, u, 2)
                if first and u < NOW:
                    sum_blocks(g, u)
                    carry(g, u)

            v.memset(parts[96:P], 0.0).then_inc(parts_zero, 1)
            dve.wait_ge(consts, CONSTS - 1)
            for u in range(U):
                tile(0, u, True)
            with dve.Fori(1, GROUPS - 1, BODY) as g:
                for i in range(BODY):
                    for u in range(U):
                        tile(g + i, u, False)
            G = GROUPS - 1
            for u in range(U):
                tile(G, u, False)
            sum_blocks(G, U - 1)
            carry(G, U - 1)
            half = G % 2
            dve.wait_ge(out_done[half], 16 * (G // 2))
            for u in range(U):
                t = G * U + u
                if u:
                    add_parts(G, u, False)
                dve.wait_ge(summed, t + 1)
                dve.wait_ge(xb_done, 1)
                dve.wait_ge(norm, NSTEPS * G)
                v.tensor_tensor(zx[:, u, :], z[:, u, :], xb[:, t, :], ALU.add).then_inc(tail, 1)
                dve.wait_ge(tail, 4 * u + 1)
                v.bn_stats(stats[:, u, :], zx[:, u, :]).then_inc(tail, 1)
                dve.wait_ge(tail, 4 * u + 2)
                v.bn_aggr(mv[:, u, :], stats[:, u, :]).then_inc(tail, 1)
                dve.wait_ge(tail, 4 * u + 3)
                dve.wait_ge(tail_pool, 2 * (u + 1))
                v.tensor_scalar(y[:, half, u, :], zx[:, u, :], mv[:, u, 0:1], rstd[:, u:u + 1], ALU.subtract,
                                ALU.mult).then_inc(tail, 1)


_INS = ['x', 'adj', 'L0_gnn_weight', 'L0_gnn_bias']
_OUTS = [((4096, 64), 'float32')]


def kernel(**inputs):
    import numpy as _np
    import concourse.bacc as _bacc
    from concourse import mybir as _mybir
    from concourse.bass_utils import run_bass_kernel_spmd as _run

    nc = _bacc.Bacc("TRN2", target_bir_lowering=False, num_devices=1)
    arrays, args = {}, []
    for name in _INS:
        a = _np.ascontiguousarray(inputs[name])
        arrays[f"in_{name}_dram"] = a
        args.append(nc.dram_tensor(f"in_{name}_dram", a.shape, _mybir.dt.from_np(a.dtype), kind="ExternalInput").ap())
    for i, (shape, dtype) in enumerate(_OUTS):
        dt = _mybir.dt.from_np(_np.dtype(dtype))
        args.append(nc.dram_tensor(f"out_{i}_dram", shape, dt, kind="ExternalOutput").ap())
    gnn_decay_resnorm_kernel(nc, *args)
    r = _run(nc, [arrays], core_ids=[0])
    return r.results[0]["out_0_dram"]
```
